# Optimizing a Trainium2 kernel written in Bass

```python
import numpy as np
import jax
import jax.numpy as jnp

def _softmax(x, axis=-1):
    return jax.nn.softmax(x, axis=axis)

def _gelu(x):
    return jax.nn.gelu(x, approximate=True)

def _silu(x):
    return jax.nn.silu(x)

def _sigmoid(x):
    return jax.nn.sigmoid(x)

def _layernorm(x, axis=-1, eps=1e-05):
    m = jnp.mean(x, axis=axis, keepdims=True)
    v = jnp.var(x, axis=axis, keepdims=True)
    return (x - m) / jnp.sqrt(v + eps)

def _scatter_add(tgt, idx, src, axis=0):
    return tgt.at[idx].add(src)

def _segment_sum(src, seg, n):
    return jax.ops.segment_sum(src, seg, n)
kernel_name = 'mk_gnn_resnorm_d2_gnn_r64_11d99d'

def setup_inputs(seed: int=0):
    np.random.seed(seed)
    _w = jnp.asarray

    def _rec_inputs():
        import jax
        import jax.numpy as jnp
        _gk = jax.random.key(seed)
        x = -0.0002117 + 1 * jax.random.normal(jax.random.fold_in(_gk, 1), (50000, 256), jnp.float32)
        src = jax.random.randint(jax.random.fold_in(_gk, 2), (25000,), 0, 50000, jnp.int32)
        dst = jax.random.randint(jax.random.fold_in(_gk, 3), (25000,), 0, 50000, jnp.int32)
        _o = jnp.argsort(dst, stable=True)
        src = src[_o]
        dst = dst[_o]
        edge_weight = jax.random.uniform(jax.random.fold_in(_gk, 12), (25000,), jnp.float32, 0.0, 0.999998)
        node_vec = jax.random.uniform(jax.random.fold_in(_gk, 13), (50000,), jnp.float32, 0.0, 0.999991)
        return (x, src, dst, edge_weight, node_vec)
    x, src, dst, edge_weight, node_vec = _rec_inputs()

    def _L0_gnn_setup():
        import jax, jax.numpy as jnp
        import numpy as np
        N = 100000
        E = 50000
        IN_DIM = 256
        OUT_DIM = 256
        EGO_DIM = OUT_DIM // 2
        NB_DIM = OUT_DIM - EGO_DIM
        key = jax.random.key(seed)
        ks = jax.random.split(key, 10)
        x = jax.random.normal(ks[0], (N, IN_DIM), dtype=jnp.float32)
        edge_index = jax.random.randint(ks[1], (2, E), 0, N, dtype=jnp.int64)
        delta_agg = jax.random.uniform(ks[2], (N,), dtype=jnp.float32)
        s = 1.0 / np.sqrt(IN_DIM)
        W_mean = jax.random.uniform(ks[3], (IN_DIM, OUT_DIM), minval=-s, maxval=s, dtype=jnp.float32)
        b_mean = jax.random.uniform(ks[4], (OUT_DIM,), minval=-s, maxval=s, dtype=jnp.float32)
        W_ego = jax.random.uniform(ks[5], (IN_DIM, EGO_DIM), minval=-s, maxval=s, dtype=jnp.float32)
        b_ego = jax.random.uniform(ks[6], (EGO_DIM,), minval=-s, maxval=s, dtype=jnp.float32)
        W_nb = jax.random.uniform(ks[7], (IN_DIM, NB_DIM), minval=-s, maxval=s, dtype=jnp.float32)
        b_nb = jax.random.uniform(ks[8], (NB_DIM,), minval=-s, maxval=s, dtype=jnp.float32)
        gate_weight = jnp.float32(1.0)
        gate_bias = jnp.float32(0.0)
        return {'x': x, 'edge_index': edge_index, 'delta_agg': delta_agg, 'W_mean': W_mean, 'b_mean': b_mean, 'W_ego': W_ego, 'b_ego': b_ego, 'W_nb': W_nb, 'b_nb': b_nb, 'gate_weight': gate_weight, 'gate_bias': gate_bias}
    _L0_gnn_all = _L0_gnn_setup()
    _L0_gnn_in = {k: v for k, v in _L0_gnn_all.items() if k in ('W_mean', 'b_mean', 'W_ego', 'b_ego', 'W_nb', 'b_nb', 'gate_weight', 'gate_bias')}
    del _L0_gnn_all

    def _L1_gnn_setup():
        import jax, jax.numpy as jnp
        import numpy as np
        N_NODES = 50000
        N_EDGES = 12500
        IN_DIM, HID_DIM, OUT_DIM, N_HEADS = (256, 256, 64, 4)
        ATT_DIM = OUT_DIM * 2 + 1
        key = jax.random.key(seed)
        ks = jax.random.split(key, 8)
        s = 0.05
        return {'x': jax.random.normal(ks[0], (N_NODES, IN_DIM), dtype=jnp.float32), 'idx': jax.random.randint(ks[1], (2, N_EDGES), 0, N_NODES, dtype=jnp.int32), 'elem': jax.random.uniform(ks[2], (N_EDGES,), dtype=jnp.float32), 'W1': jax.random.normal(ks[3], (N_HEADS, IN_DIM, HID_DIM), dtype=jnp.float32) * s, 'b1': jnp.zeros((N_HEADS, HID_DIM), jnp.float32), 'W2': jax.random.normal(ks[4], (N_HEADS, HID_DIM, OUT_DIM), dtype=jnp.float32) * s, 'b2': jnp.zeros((N_HEADS, OUT_DIM), jnp.float32), 'A1': jax.random.normal(ks[5], (N_HEADS, ATT_DIM, ATT_DIM), dtype=jnp.float32) * s, 'ab1': jnp.zeros((N_HEADS, ATT_DIM), jnp.float32), 'A2': jax.random.normal(ks[6], (N_HEADS, ATT_DIM, 1), dtype=jnp.float32) * s, 'ab2': jnp.zeros((N_HEADS, 1), jnp.float32)}
    _L1_gnn_all = _L1_gnn_setup()
    _L1_gnn_in = {k: v for k, v in _L1_gnn_all.items() if k in ('W1', 'b1', 'W2', 'b2', 'A1', 'ab1', 'A2', 'ab2')}
    del _L1_gnn_all
    return {'x': x, 'src': src, 'dst': dst, 'edge_weight': edge_weight, 'node_vec': node_vec, 'L0_gnn_W_mean': _L0_gnn_in['W_mean'], 'L0_gnn_b_mean': _L0_gnn_in['b_mean'], 'L0_gnn_W_ego': _L0_gnn_in['W_ego'], 'L0_gnn_b_ego': _L0_gnn_in['b_ego'], 'L0_gnn_W_nb': _L0_gnn_in['W_nb'], 'L0_gnn_b_nb': _L0_gnn_in['b_nb'], 'L0_gnn_gate_weight': _L0_gnn_in['gate_weight'], 'L0_gnn_gate_bias': _L0_gnn_in['gate_bias'], 'L1_gnn_W1': _L1_gnn_in['W1'], 'L1_gnn_b1': _L1_gnn_in['b1'], 'L1_gnn_W2': _L1_gnn_in['W2'], 'L1_gnn_b2': _L1_gnn_in['b2'], 'L1_gnn_A1': _L1_gnn_in['A1'], 'L1_gnn_ab1': _L1_gnn_in['ab1'], 'L1_gnn_A2': _L1_gnn_in['A2'], 'L1_gnn_ab2': _L1_gnn_in['ab2']}

def reference(x, src, dst, edge_weight, node_vec, L0_gnn_W_mean, L0_gnn_b_mean, L0_gnn_W_ego, L0_gnn_b_ego, L0_gnn_W_nb, L0_gnn_b_nb, L0_gnn_gate_weight, L0_gnn_gate_bias, L1_gnn_W1, L1_gnn_b1, L1_gnn_W2, L1_gnn_b2, L1_gnn_A1, L1_gnn_ab1, L1_gnn_A2, L1_gnn_ab2):
    import jax
    import jax.numpy as jnp

    def _L0_gnn_ref(x, edge_index, delta_agg, W_mean, b_mean, W_ego, b_ego, W_nb, b_nb, gate_weight, gate_bias):
        import jax, jax.numpy as jnp
        import numpy as np
        N = 100000
        E = 50000
        IN_DIM = 256
        OUT_DIM = 256
        EGO_DIM = OUT_DIM // 2
        NB_DIM = OUT_DIM - EGO_DIM
        n = x.shape[0]
        row, col = (edge_index[0], edge_index[1])
        neighbor_sum = jax.ops.segment_sum(x[col], row, num_segments=n)
        deg = jax.ops.segment_sum(jnp.ones((row.shape[0],), dtype=x.dtype), row, num_segments=n)
        deg = jnp.maximum(deg, 1.0)
        mean_neighbor = neighbor_sum / deg[:, None]
        h_mean = (x + mean_neighbor) * 0.5 @ W_mean + b_mean
        h_ego = x @ W_ego + b_ego
        h_neighbor = mean_neighbor @ W_nb + b_nb
        h_concat = jnp.concatenate([h_ego, h_neighbor], axis=1)
        gate = jax.nn.sigmoid(gate_weight * delta_agg + gate_bias)[:, None]
        return (1.0 - gate) * h_mean + gate * h_concat

    def _L1_gnn_ref(x, idx, elem, W1, b1, W2, b2, A1, ab1, A2, ab2):
        import jax, jax.numpy as jnp
        import numpy as np
        N_NODES = 50000
        N_EDGES = 12500
        IN_DIM, HID_DIM, OUT_DIM, N_HEADS = (256, 256, 64, 4)
        ATT_DIM = OUT_DIM * 2 + 1
        row, col = (idx[0], idx[1])
        n = x.shape[0]

        def head(w1, bb1, w2, bb2, a1, aab1, a2, aab2):
            feats = jnp.maximum(x @ w1 + bb1, 0.0) @ w2 + bb2
            x_cat = jnp.concatenate([feats[row], feats[col], elem[:, None]], axis=1)
            hid = jnp.maximum(x_cat @ a1 + aab1, 0.0)
            e1 = (hid @ a2 + aab2)[:, 0]
            e1 = jax.nn.leaky_relu(e1, negative_slope=0.2)
            w = jnp.exp(e1 - jnp.max(e1))
            pooled = jax.ops.segment_sum(w[:, None] * feats[col], row, num_segments=n)
            row_sum = jax.ops.segment_sum(w, row, num_segments=n) + 1e-10
            return pooled / row_sum[:, None]
        h = jax.vmap(head)(W1, b1, W2, b2, A1, ab1, A2, ab2)
        return jnp.transpose(h, (1, 0, 2)).reshape(n, -1)
    edge_index = jnp.stack([src, dst])
    x = _layernorm(x + _L0_gnn_ref(x, edge_index, node_vec, L0_gnn_W_mean, L0_gnn_b_mean, L0_gnn_W_ego, L0_gnn_b_ego, L0_gnn_W_nb, L0_gnn_b_nb, L0_gnn_gate_weight, L0_gnn_gate_bias), axis=-1)
    x = _layernorm(x + _L1_gnn_ref(x, edge_index, edge_weight, L1_gnn_W1, L1_gnn_b1, L1_gnn_W2, L1_gnn_b2, L1_gnn_A1, L1_gnn_ab1, L1_gnn_A2, L1_gnn_ab2), axis=-1)
    return x

_drawn_inputs = setup_inputs


def setup_inputs(seed=0):
    import zlib

    import numpy as np

    out = dict(_drawn_inputs(seed))
    spreads = {'L1_gnn_b1': (0.0, 0.1),
     'L1_gnn_b2': (0.0, 0.1),
     'L1_gnn_ab1': (0.0, 2.0),
     'L1_gnn_ab2': (0.0, 2.0)}
    factors = {'edge_weight': 8.0,
     'L0_gnn_b_mean': 4.329,
     'L0_gnn_b_ego': 3.593,
     'L0_gnn_b_nb': 3.579,
     'L1_gnn_A1': 8.0,
     'L1_gnn_A2': 8.0}
    for name, (base, spread) in spreads.items():
        noise = np.random.default_rng([zlib.crc32(name.encode()), seed]).standard_normal(out[name].shape)
        drawn = base * np.exp(spread * noise) if base else spread * noise
        out[name] = jnp.asarray(drawn.astype(out[name].dtype))
    for name, factor in factors.items():
        out[name] = (out[name] * factor).astype(out[name].dtype)
    return out
```

```python
import numpy as np
import concourse.bass as bass
from concourse import mybir
from contextlib import ExitStack

F32, F32R, F16 = mybir.dt.float32, mybir.dt.float32r, mybir.dt.float16
BF16, I32 = mybir.dt.bfloat16, mybir.dt.int32
ALU, ACT = mybir.AluOpType, mybir.ActivationFunctionType
AX = mybir.AxisListType
P, D = 128, 256
HEADS, HID, FEAT = 4, 256, 64
ATT = 2 * FEAT + 1
EPS = 1e-5
HALF = 5
LO = 512
CHUNK = 4


class Steps:

    def __init__(self, eng, sem):
        self.eng, self.sem, self.base, self.n = eng, sem, 0, 0

    def done(self, ins):
        ins.then_inc(self.sem, 1)
        self.n += 1

    def wait(self, back=0):
        self.eng.wait_ge(self.sem, self.base + (self.n - back))

    def loop(self, n, body):
        first = self.base + self.n
        body(0)
        per = self.base + self.n - first
        if n > 1:
            with self.eng.Fori(1, n) as j:
                self.base, self.n = j * per + first, 0
                body(j)
                assert self.n == per
        self.base, self.n = first + n * per, 0


def later(j):
    return not isinstance(j, int) or j > 0


def skewed(eng, n, unroll, stages):
    def step(j, q):
        for fn, lag in stages:
            t = j * unroll + (q - lag)
            if not isinstance(t, int) or 0 <= t < n:
                fn(t, (q - lag) % unroll)

    rounds, left = n // unroll, n % unroll
    for j in range(min(2, rounds)):
        for q in range(unroll):
            step(j, q)
    if rounds > 2:
        with eng.Fori(2, rounds) as j:
            for q in range(unroll):
                step(j, q)
    for q in range(left + max(lag for _, lag in stages)):
        step(rounds, q)


def after(t, k):
    return not isinstance(t, int) or t >= k


def row1(ap):
    return ap.unsqueeze(0)


def build(nc, x, src, dst, edge_weight, node_vec, W_mean, b_mean, W_ego, b_ego, W_nb, b_nb, gate_weight,
          gate_bias, W1, b1, W2, b2, A1, ab1, A2, ab2, out):
    N, E = x.shape[0], src.shape[0]
    NT = N // P
    ITER = NT // (2 * HALF)
    assert ITER * 2 * HALF == NT
    EC, ER = E // P, E % P
    ET = EC + 1
    assert ER and ET % CHUNK == 0 and ET % 2 == 0
    HI = (N >> 9) + 1
    assert HI <= P
    NCH = ET // CHUNK
    PAD = float(1 << 17)
    with ExitStack() as ctx:
        def sb(n, s, d=F32):
            return ctx.enter_context(nc.sbuf_tensor(n, s, d))

        def sem(n):
            return ctx.enter_context(nc.semaphore(n))

        part = [ExitStack()]

        def tmp(n, s, d=F32):
            return part[0].enter_context(nc.sbuf_tensor(n, s, d))

        def give_back():
            part[0].close()
            part[0] = ExitStack()

        bank = [ctx.enter_context(nc.psum_tensor(f"bank{i}", [P, 512], F32)) for i in range(8)]
        h_tab = nc.dram_tensor("h_tab", [N, D], F32).ap()
        rec_tab = nc.dram_tensor("rec_tab", [P * ET, 4], F32).ap()
        edge_tab = nc.dram_tensor("edge_tab", [ET, P, 2 * D], F32).ap()

        ident = sb("ident", [P, P])
        iota_hi = sb("iota_hi", [P, P], F16)
        iota_p = sb("iota_p", [P, 1])
        below = sb("below", [P, P])
        is127 = sb("is127", [P, 1])
        ones3 = sb("ones3", [3, P], BF16)
        NB = 512
        AB = HEADS * ATT
        bias3 = sb("bias3", [3, NB + AB], BF16)
        gwb = sb("gwb", [P, 2])
        w_node = sb("w_node", [P, 2, 384])
        w_nb = sb("w_nb", [P, 2, 384])
        w1h = sb("w1h", [P, 2, HEADS * HID], F32R)
        w1l = sb("w1l", [P, 2, HEADS * HID], F32R)
        b1c = sb("b1c", [P, 2 * HEADS])
        b2c = sb("b2c", [P, HEADS])
        w2f = sb("w2f", [P, 2 * HEADS, FEAT])
        a1f = sb("a1f", [P, HEADS, ATT])
        a1e = sb("a1e", [P, AB])
        a2b = sb("a2b", [P, AB])
        ab2b = sb("ab2b", [P, HEADS])
        rec = sb("rec", [P, ET, 4])
        idx_u = sb("idx_u", [P, ET], I32)
        tmp_i = sb("tmp_i", [P, 2, ET], I32)
        pos = sb("pos", [P, ET])
        nxt = sb("nxt", [P, ET, 4])
        idx_s = sb("idx_s", [P, ET, 4], I32)
        key1 = sb("key1", [P, ET])
        prev1 = sb("prev1", [P, ET])
        gate_e = sb("gate_e", [P, ET, 2])
        score = sb("score", [P, ET, HEADS])
        wgt = sb("wgt", [P, ET, HEADS])
        nv = sb("nv", [P, NT + 1])
        gate_n = sb("gate_n", [P, NT + 1])
        omg_n = sb("omg_n", [P, NT + 1])

        in_sem = sem("inputs_loaded")
        const_ready = sem("const_ready")
        bias_row = tmp("bias_row", [1, NB + AB])
        bias_res = tmp("bias_res", [1, NB + AB])
        bias_part = tmp("bias_part", [1, 3, NB + AB], BF16)
        w1f = tmp("w1f", [P, 2, HEADS * HID])
        iota_lof = tmp("iota_lof", [P, LO])
        earlier = tmp("earlier", [P, CHUNK * P])
        iota_lo = tmp("iota_lo", [P, LO], F16)
        keys = tmp("keys", [P, 3, ET])
        s_bias = sem("bias_parts")
        s_bias3 = sem("bias3_loaded")
        nv_idx = tmp("nv_idx", [P, 2, CHUNK], I32)
        nv_got = tmp("nv_got", [P, 2, CHUNK])
        oh_hi = tmp("oh_hi", [P, CHUNK, P], F16)
        oh_lo = tmp("oh_lo", [P, CHUNK, LO], F16)
        hist = tmp("hist", [P, LO])
        scan = tmp("scan", [P, 2, LO])
        G = tmp("G", [P, LO])
        g_big = tmp("g_big", [P, LO], F16)
        g_small = tmp("g_small", [P, LO], F16)
        keys4 = tmp("keys4", [P, 2, CHUNK])
        ohT = tmp("ohT", [P, CHUNK * P], F16)
        junk = tmp("junk", [P, 2 * CHUNK, LO])
        bin0 = tmp("bin0", [P, 2])
        sel = tmp("sel", [P, CHUNK])
        rank = tmp("rank", [P, CHUNK])
        dve1 = sem("dve1")
        act1 = sem("act1")
        oh_ready, oh_used = sem("oh_ready"), sem("oh_used")
        base_in, base_out = sem("base_in"), sem("base_out")
        keys_ready, keysT_ready = sem("keys_ready"), sem("keysT_ready")
        ohT_ready, look_ready, look_used = sem("ohT_ready"), sem("look_ready"), sem("look_used")
        oh2_ready, hist2_ready = sem("oh2_ready"), sem("hist2_ready")
        g_ready = sem("g_ready")
        nvi_ready, nv_taken = sem("nvi_ready"), sem("nv_taken")
        nv_in = [sem(f"nv_in{b}") for b in range(2)]
        rec_ready = sem("rec_ready")
        pool_hop, dve_hop = sem("pool_hop"), sem("dve_hop")
        pc = [0]

        with nc.Block() as block:
            @block.sync
            def _(sp):
                n = [0]

                def load(dst_, src_):
                    sp.dma_start(dst_, src_).then_inc(in_sem, 16)
                    n[0] += 1

                sp.wait_ge(const_ready, 1)
                load(tmp_i[:, 0, 0:EC], src[0:P * EC].rearrange("(p t) -> p t", p=P))
                load(tmp_i[0:ER, 0, EC:ET], src[P * EC:E].unsqueeze(1))
                load(tmp_i[:, 1, 0:EC], dst[0:P * EC].rearrange("(p t) -> p t", p=P))
                load(tmp_i[0:ER, 1, EC:ET], dst[P * EC:E].unsqueeze(1))
                load(pos[:, 0:EC], edge_weight[0:P * EC].rearrange("(p t) -> p t", p=P))
                load(pos[0:ER, EC:ET], edge_weight[P * EC:E].unsqueeze(1))
                load(nv[:, 0:NT], node_vec[0:P * NT].rearrange("(p t) -> p t", p=P))
                load(nv[:, NT:NT + 1], node_vec[N - P:N].unsqueeze(1))
                load(gwb[:, 0:1], gate_weight.partition_broadcast(P))
                load(gwb[:, 1:2], gate_bias.partition_broadcast(P))
                for w, o in ((W_mean, 0), (W_ego, 256)):
                    load(w_node[:, :, o:o + w.shape[1]], w.rearrange("(c k) m -> k c m", k=P))
                load(w_nb[:, :, 256:384], W_nb.rearrange("(c k) m -> k c m", k=P))
                for c in range(2):
                    load(w1f[:, c, :].rearrange("k (h m) -> k h m", h=HEADS),
                         W1[:, c * P:(c + 1) * P, :].rearrange("h k m -> k h m"))
                with nc.allow_non_contiguous_dma(reason="1024 biases, once"):
                    for h in range(HEADS):
                        load(b1c[:, 2 * h:2 * h + 2], b1[h].rearrange("(c p) -> p c", p=P))
                for h in range(HEADS):
                    load(w2f[:, 2 * h:2 * h + 2, :], W2[h].rearrange("(c k) m -> k c m", k=P))
                load(a1f[:, :, :], A1[:, 0:P, :].rearrange("h k m -> k h m"))
                for h in range(HEADS):
                    load(a1e[:, h * ATT:(h + 1) * ATT], A1[h, P, :].partition_broadcast(P))
                    load(a2b[:, h * ATT:(h + 1) * ATT], A2[h, :, 0].partition_broadcast(P))
                    load(bias_row[:, NB + h * ATT:NB + (h + 1) * ATT], row1(ab1[h]))
                with nc.allow_non_contiguous_dma(reason="512 biases, once"):
                    for s in range(2):
                        load(b2c[s * FEAT:(s + 1) * FEAT, :], b2.rearrange("h f -> f h"))
                load(ab2b[:, :], ab2.rearrange("h a -> (h a)").partition_broadcast(P))
                load(bias_row[:, 0:256], row1(b_mean))
                load(bias_row[:, 256:384], row1(b_ego))
                load(bias_row[:, 384:512], row1(b_nb))
                pc[0] = 16 * n[0]
                sp.wait_ge(s_bias, 1)
                for k in range(3):
                    sp.dma_start(bias3[k:k + 1, :], bias_part[:, k, :]).then_inc(s_bias3, 16)
                sp.wait_ge(s_bias3, 48)

            loaded = pc[0]

            @block.gpsimd
            def _(pool):
                g = nc.gpsimd
                hop = Steps(pool, pool_hop)
                hop.done(g.memset(pos[:, :], 0.0))
                hop.done(g.iota(tmp_i[:, 0, :], pattern=[[0, ET]], base=N, channel_multiplier=0))
                hop.done(g.iota(tmp_i[:, 1, :], pattern=[[0, ET]], base=0, channel_multiplier=0))
                hop.wait()
                pool.sem_inc(const_ready, 1)
                hop.done(g.iota(iota_lo[:, :], pattern=[[1, LO]], base=0, channel_multiplier=0,
                                allow_small_or_imprecise_dtypes=True))
                hop.done(g.iota(iota_lof[:, :], pattern=[[1, LO]], base=0, channel_multiplier=0,
                                allow_small_or_imprecise_dtypes=True))
                hop.done(g.iota(iota_hi[:, :], pattern=[[1, P]], base=0, channel_multiplier=0,
                                allow_small_or_imprecise_dtypes=True))
                hop.done(g.iota(iota_p[:, :], pattern=[[0, 1]], base=0, channel_multiplier=1,
                                allow_small_or_imprecise_dtypes=True))
                for t in (ident, below, earlier):
                    hop.done(g.memset(t[:, :], 0.0 if t is ident else 1.0))
                hop.done(g.memset(is127[:, :], 0.0))
                hop.done(g.memset(ones3[:, :], 1.0))
                hop.wait()
                hop.done(g.affine_select(out=ident[:, :], in_=ident[:, :], compare_op=ALU.not_equal, fill=1.0,
                                         base=0, pattern=[[-1, P]], channel_multiplier=1))
                hop.done(g.affine_select(out=below[:, :], in_=below[:, :], compare_op=ALU.is_gt, fill=0.0,
                                         base=0, pattern=[[1, P]], channel_multiplier=-1))
                hop.done(g.affine_select(out=earlier[:, :], in_=earlier[:, :], compare_op=ALU.is_gt, fill=0.0,
                                         base=(CHUNK - 1) * P, pattern=[[-1, CHUNK * P]], channel_multiplier=1))
                hop.done(g.affine_select(out=is127[:, :], in_=is127[:, :], compare_op=ALU.not_equal, fill=1.0,
                                         base=-(P - 1), pattern=[[0, 1]], channel_multiplier=1))
                hop.wait()
                pool.sem_inc(const_ready, 1)
                last = pool.to_reg(N - 1)

                def gather(c, b):
                    pool.wait_ge(nvi_ready, c + 1)
                    pool.sem_inc(pool_hop, 1)
                    for q in range(CHUNK):
                        g.indirect_dma_start(
                            out=nv_got[:, b, q:q + 1], out_offset=None, in_=node_vec.unsqueeze(1),
                            in_offset=bass.IndirectOffsetOnAxis(nv_idx[:, b, q:q + 1], 0),
                            bounds_check=last, oob_is_err=False).then_inc(nv_in[b], 16)

                skewed(pool, NCH, 2, [(gather, 0)])
                for b in range(2):
                    pool.wait_ge(nv_in[b], len(range(b, NCH, 2)) * CHUNK * 16)

            @block.scalar
            def _(act):
                st = Steps(act, act1)
                act.wait_ge(in_sem, loaded)
                st.done(nc.scalar.activation(gate_n[:, :], nv[:, :], ACT.Sigmoid, bias=gwb[:, 1:2], scale=gwb[:, 0:1]))
                st.wait()
                st.done(nc.scalar.activation(omg_n[:, :], gate_n[:, :], ACT.Copy, bias=1.0, scale=-1.0))
                st.done(nc.scalar.activation(w1h[:, :, :], w1f[:, :, :], ACT.Copy))

            @block.vector
            def _(dve):
                v = nc.vector
                st = Steps(dve, dve1)
                dve.wait_ge(in_sem, loaded)
                dve.wait_ge(const_ready, 2)
                st.done(v.tensor_copy(rec[:, :, 0], tmp_i[:, 0, :]))
                st.done(v.tensor_copy(rec[:, :, 1], tmp_i[:, 1, :]))
                st.done(v.tensor_copy(rec[:, :, 2], pos[:, :]))
                st.done(v.tensor_copy(keys[:, 0, :], tmp_i[:, 0, :]))
                st.wait()
                st.done(v.memset(rec[:, :, 3], 0.0))
                st.done(v.memset(nv_got[:, :, :], 0.0))
                st.done(v.tensor_single_scalar(idx_u[:, :], tmp_i[:, 0, :], LO - 1, ALU.bitwise_and))
                st.done(v.tensor_single_scalar(tmp_i[:, 1, :], tmp_i[:, 0, :], 9, ALU.arith_shift_right))
                st.wait()
                st.done(v.tensor_copy(keys[:, 1, :], tmp_i[:, 1, :]))
                st.done(v.tensor_copy(keys[:, 2, :], idx_u[:, :]))
                st.done(v.tensor_scalar(w_node[:, :, 0:256], w_node[:, :, 0:256], 0.5, None, ALU.mult))
                st.wait()
                st.done(v.tensor_copy(w_nb[:, :, 0:256], w_node[:, :, 0:256]))
                dve.wait_ge(act1, 3)
                st.done(v.tensor_tensor(w1l[:, :, :], w1f[:, :, :], w1h[:, :, :].bitcast(F32), ALU.subtract))
                st.done(v.tensor_copy(bias_part[:, 0, :], bias_row[:, :]))
                st.wait()
                st.done(v.tensor_tensor(bias_res[:, :], bias_row[:, :], bias_part[:, 0, :], ALU.subtract))
                st.wait()
                st.done(v.tensor_copy(bias_part[:, 1, :], bias_res[:, :]))
                st.wait()
                st.done(v.tensor_tensor(bias_row[:, :], bias_res[:, :], bias_part[:, 1, :], ALU.subtract))
                st.wait()
                v.tensor_copy(bias_part[:, 2, :], bias_row[:, :]).then_inc(s_bias, 1)

                def onehots(j, ready):
                    if later(j):
                        dve.wait_ge(oh_used if ready is oh_ready else hist2_ready, j)
                    for q in range(CHUNK):
                        t = j * CHUNK + q
                        v.tensor_scalar(oh_hi[:, q, 0:HI], iota_hi[:, 0:HI], keys[:, 1, bass.ds(t, 1)], None,
                                        ALU.is_equal)
                        v.tensor_scalar(oh_lo[:, q, :], iota_lo[:, :], keys[:, 2, bass.ds(t, 1)], None,
                                        ALU.is_equal).then_inc(ready, 1)

                def take_nv(c, b):
                    dve.wait_ge(nv_in[b], (c - b) * (CHUNK * 8) + CHUNK * 16)
                    v.tensor_copy(rec[:, bass.ds(c * CHUNK, CHUNK), 3], nv_got[:, b, :]).then_inc(nv_taken, 1)

                def count(c, b):
                    onehots(c, oh_ready)
                    if after(c, 2):
                        take_nv(c - 2, b)
                        dve.wait_ge(nv_taken, c - 1)
                    v.tensor_copy(nv_idx[:, b, :], tmp_i[:, 0, bass.ds(c * CHUNK, CHUNK)]).then_inc(nvi_ready, 1)

                skewed(dve, NCH, 2, [(count, 0)])
                for c in (NCH - 2, NCH - 1):
                    take_nv(c, c % 2)
                dve.wait_ge(oh_used, ET // CHUNK)
                st.done(v.tensor_copy(hist[0:HI, :], bank[0][0:HI, :]))
                st.done(v.tensor_copy(scan[0:HI, 0, :], bank[0][0:HI, :]))
                a, step = 0, 1
                while step < LO:
                    st.wait()
                    st.done(v.tensor_tensor(scan[0:HI, 1 - a, step:], scan[0:HI, a, step:], scan[0:HI, a, :LO - step],
                                            ALU.add))
                    st.done(v.tensor_copy(scan[0:HI, 1 - a, 0:step], scan[0:HI, a, 0:step]))
                    a, step = 1 - a, step * 2
                st.wait()
                st.done(v.tensor_copy(bin0[0:HI, 0:1], scan[0:HI, a, LO - 1:LO]))
                st.wait()
                dve.sem_inc(base_in, 1)
                st.done(v.tensor_tensor(scan[0:HI, 1 - a, :], scan[0:HI, a, :], hist[0:HI, :], ALU.subtract))
                dve.wait_ge(base_out, 1)
                st.done(v.tensor_copy(bin0[0:HI, 1:2], bank[1][0:HI, 0:1]))
                st.wait()
                st.done(v.tensor_scalar(G[0:HI, :], scan[0:HI, 1 - a, :], bin0[0:HI, 1:2], None, ALU.add))
                st.wait()
                st.done(v.tensor_copy(g_big[0:HI, :], G[0:HI, :]))
                st.wait()
                st.done(v.tensor_tensor(g_small[0:HI, :], G[0:HI, :], g_big[0:HI, :], ALU.subtract))
                st.wait()
                dve.sem_inc(g_ready, 1)

                def place(j):
                    if later(j):
                        dve.wait_ge(keysT_ready, j)
                    st.done(v.tensor_copy(keys4[:, :, :], keys[:, 0:2, bass.ds(j * CHUNK, CHUNK)]))
                    st.wait()
                    dve.sem_inc(keys_ready, 1)
                    onehots(j, oh2_ready)
                    dve.wait_ge(keysT_ready, j + 1)
                    if later(j):
                        dve.wait_ge(look_ready, j * CHUNK)
                    v.tensor_scalar(ohT[0:HI, :], bank[3][0:HI, :], iota_p[0:HI, :], None, ALU.is_equal)\
                        .then_inc(ohT_ready, 1)
                    for q in range(CHUNK):
                        w = P * (q + 1)
                        v.scalar_tensor_tensor(out=junk[:, q, 0:w], in0=bank[2][:, 0:w],
                                               scalar=keys4[:, 0, q:q + 1],
                                               in1=earlier[:, CHUNK * P - w:CHUNK * P], op0=ALU.is_equal,
                                               op1=ALU.mult, accum_out=rank[:, q:q + 1])
                    for q in range(CHUNK):
                        dve.wait_ge(look_ready, j * CHUNK + (q + 1))
                        ins = v.scalar_tensor_tensor(out=junk[:, CHUNK + q, :], in0=iota_lof[:, :],
                                                     scalar=keys[:, 2, bass.ds(j * CHUNK + q, 1)],
                                                     in1=bank[4 + q % 2][:, :], op0=ALU.is_equal, op1=ALU.mult,
                                                     accum_out=sel[:, q:q + 1])
                        ins.then_inc(look_used, 1)
                    dve.wait_ge(look_used, j * CHUNK + CHUNK)
                    dve.wait_ge(hist2_ready, j + 1)
                    st.done(v.tensor_tensor(pos[:, bass.ds(j * CHUNK, CHUNK)], sel[:, :], rank[:, :], ALU.add))
                    st.done(v.tensor_tensor(G[0:HI, :], G[0:HI, :], bank[6][0:HI, :], ALU.add))
                    st.wait()
                    st.done(v.tensor_copy(g_big[0:HI, :], G[0:HI, :]))
                    st.wait()
                    v.tensor_tensor(g_small[0:HI, :], G[0:HI, :], g_big[0:HI, :], ALU.subtract).then_inc(g_ready, 1)

                st.loop(ET // CHUNK, place)
                dve.wait_ge(g_ready, ET // CHUNK + 1)
                st.done(v.tensor_copy(tmp_i[:, 0, :], pos[:, :]))
                st.wait()
                st.done(v.tensor_single_scalar(tmp_i[:, 1, :], tmp_i[:, 0, :], 7, ALU.arith_shift_right))
                st.done(v.tensor_single_scalar(idx_u[:, :], tmp_i[:, 0, :], P - 1, ALU.bitwise_and))
                st.wait()
                st.done(v.tensor_copy(pos[:, :], idx_u[:, :]))
                st.done(v.tensor_copy(keys[:, 0, :], tmp_i[:, 1, :]))
                st.wait()
                st.done(v.scalar_tensor_tensor(out=pos[:, :], in0=pos[:, :], scalar=float(ET), in1=keys[:, 0, :],
                                               op0=ALU.mult, op1=ALU.add))
                st.wait()
                st.done(v.tensor_copy(idx_u[:, :], pos[:, :]))
                st.wait()
                dve.sem_inc(rec_ready, 1)

            @block.tensor
            def _(pe):
                t = nc.tensor

                def count(j, start, stop):
                    for q in range(CHUNK):
                        pe.wait_ge(oh_ready, j * CHUNK + (q + 1))
                        ins = t.matmul(bank[0][0:HI, :], oh_hi[:, q, 0:HI], oh_lo[:, q, :], start=start and q == 0,
                                       stop=stop and q == CHUNK - 1, skip_group_check=True)
                    ins.then_inc(oh_used, 1)

                count(0, True, False)
                with pe.Fori(1, NCH - 1) as j:
                    count(j, False, False)
                count(NCH - 1, False, True)
                pe.wait_ge(base_in, 1)
                t.matmul(bank[1][0:HI, 0:1], below[0:HI, 0:HI], bin0[0:HI, 0:1], start=True, stop=True)\
                    .then_inc(base_out, 1)

                def place(j):
                    pe.wait_ge(keys_ready, j + 1)
                    if later(j):
                        pe.wait_ge(look_used, j * CHUNK)
                    for q in range(CHUNK):
                        for k in range(2):
                            ins = t.transpose(bank[2 + k][:, q * P:(q + 1) * P],
                                              keys4[:, k, q:q + 1].to_broadcast([P, P]), ident[:, :])
                    ins.then_inc(keysT_ready, 1)
                    for q in range(CHUNK):
                        pe.wait_ge(oh2_ready, j * CHUNK + (q + 1))
                        if q == 0:
                            pe.wait_ge(g_ready, j + 1)
                        ins = t.matmul(bank[6][0:HI, :], oh_hi[:, q, 0:HI], oh_lo[:, q, :], start=q == 0,
                                       stop=q == CHUNK - 1)
                    ins.then_inc(hist2_ready, 1)
                    pe.wait_ge(ohT_ready, j + 1)
                    for q in range(CHUNK):
                        if q > 1:
                            pe.wait_ge(look_used, j * CHUNK + (q - 1))
                        for part in (g_big, g_small):
                            ins = t.matmul(bank[4 + q % 2][:, :], ohT[0:HI, q * P:(q + 1) * P], part[0:HI, :],
                                           start=part is g_big, stop=part is g_small)
                        ins.then_inc(look_ready, 1)

                place(0)
                with pe.Fori(1, NCH) as j:
                    place(j)

        give_back()

        TEN = 2 * HALF
        X = [tmp(f"X{s}", [P, HALF, D]) for s in range(2)]
        H = [tmp(f"H{s}", [P, HALF, D]) for s in range(2)]
        O = [tmp(f"O{s}", [P, HALF, D]) for s in range(2)]
        xT = [tmp(f"xT{b}", [P, D]) for b in range(2)]
        stats = tmp("stats", [P, TEN, 6])
        mv = tmp("mv", [P, TEN, 2])
        var_s = tmp("var_s", [P, TEN])
        sd_s = tmp("sd_s", [P, TEN])
        r_s = tmp("r_s", [P, TEN])
        nb_s = tmp("nb_s", [P, TEN])
        x_in = [sem(f"x_in{s}") for s in range(2)]
        h_out = [sem(f"h_out{s}") for s in range(2)]
        o_out = [sem(f"o_out{s}") for s in range(2)]
        xt_ready, xt_copied, p_ready = sem("xt_ready"), sem("xt_copied"), sem("p_ready")
        a_done, h_done, s_done = sem("a_done"), sem("h_done"), sem("s_done")
        mv_done, var_ready, sd_ready, r_done, nb_ready, o_done = (sem(n) for n in (
            "mv_done", "var_ready", "sd_ready", "r_done", "nb_ready", "o_done"))
        rec_slot = tmp("rec_slot", [P, 2, 4])
        idx_slot = tmp("idx_slot", [P, 2], I32)
        slot_full = sem("slot_full")
        rec_out = [sem(f"rec_out{b}") for b in range(2)]
        x_main = x[0:P * NT].rearrange("(p t) d -> p t d", p=P)
        h_main = h_tab[0:P * NT].rearrange("(p t) d -> p t d", p=P)
        o_main = out[0:P * NT].rearrange("(p t) d -> p t d", p=P)

        with nc.Block() as block:
            @block.sync
            def _(sp):
                def load(j, s):
                    sp.dma_start(X[s][:, :, :], x_main[:, bass.ds(j * TEN + s * HALF, HALF), :])\
                        .then_inc(x_in[s], 16)

                def store(j, s):
                    sp.wait_ge(h_done, j * TEN + (s + 1) * HALF)
                    sp.dma_start(h_main[:, bass.ds(j * TEN + s * HALF, HALF), :], H[s][:, :, :])\
                        .then_inc(h_out[s], 16)

                def store_o(j, s):
                    sp.wait_ge(o_done, j * TEN + (s + 1) * HALF)
                    sp.dma_start(o_main[:, bass.ds(j * TEN + s * HALF, HALF), :], O[s][:, :, :])\
                        .then_inc(o_out[s], 16)

                load(0, 0)
                load(0, 1)
                with sp.Fori(0, ITER - 1) as j:
                    for s in range(2):
                        store(j, s)
                        load(j + 1, s)
                        store_o(j, s)
                store(ITER - 1, 0)
                sp.dma_start(X[0][:, 0, :], x[N - P:N]).then_inc(x_in[0], 16)
                store_o(ITER - 1, 0)
                store(ITER - 1, 1)
                store_o(ITER - 1, 1)
                for s in range(2):
                    sp.wait_ge(h_out[s], 16 * ITER)
                    sp.wait_ge(o_out[s], 16 * ITER)
                sp.wait_ge(h_done, NT + 1)
                sp.dma_start(h_tab[N - P:N], H[0][:, 0, :]).then_inc(h_out[0], 16)
                sp.wait_ge(o_done, NT + 1)
                sp.dma_start(out[N - P:N], O[0][:, 0, :]).then_inc(o_out[0], 16)
                sp.wait_ge(h_out[0], 16 * ITER + 16)
                sp.wait_ge(o_out[0], 16 * ITER + 16)

            @block.gpsimd
            def _(pool):
                g = nc.gpsimd

                def place(t, b):
                    if after(t, 2):
                        pool.wait_ge(rec_out[b], (t - b) * 8)
                    pool.sem_inc(pool_hop, 1)
                    g.tensor_copy(rec_slot[:, b, :], rec[:, bass.ds(t, 1), :]).then_inc(slot_full, 1)
                    g.tensor_copy(idx_slot[:, b:b + 1], idx_u[:, bass.ds(t, 1)]).then_inc(slot_full, 1)
                    pool.wait_ge(slot_full, t * 2 + 2)
                    pool.sem_inc(pool_hop, 1)
                    g.indirect_dma_start(out=rec_tab, out_offset=bass.IndirectOffsetOnAxis(idx_slot[:, b:b + 1], 0),
                                         in_=rec_slot[:, b, :], in_offset=None).then_inc(rec_out[b], 16)

                skewed(pool, ET, 2, [(place, 0)])
                for b in range(2):
                    pool.wait_ge(rec_out[b], 8 * ET)

            @block.scalar
            def _(act):
                a = nc.scalar

                def copy_x(t, i):
                    act.wait_ge(xt_ready, t + 1)
                    if after(t, 2):
                        act.wait_ge(p_ready, t - 1)
                    a.activation(xT[i % 2][:, :], bank[i % 2][:, 0:D], ACT.Copy).then_inc(xt_copied, 1)

                def root(t0, s, n):
                    act.wait_ge(var_ready, t0 + 1)
                    a.activation(sd_s[:, s * HALF:s * HALF + n], var_s[:, s * HALF:s * HALF + n], ACT.Sqrt)\
                        .then_inc(sd_ready, 1)

                def norm(t, half, i):
                    s, k = i // HALF, i % HALF
                    act.wait_ge(nb_ready, half + 1)
                    if after(t, TEN) and k == 0:
                        act.wait_ge(o_out[s], (half - s) * 8)
                    a.activation(O[s][:, k, :], H[s][:, k, :], ACT.Identity, bias=nb_s[:, i:i + 1],
                                 scale=r_s[:, i:i + 1]).then_inc(o_done, 1)

                def round_(j):
                    for i in range(TEN + 1):
                        if i < TEN:
                            copy_x(j * TEN + i, i)
                        if later(j):
                            if i == 1:
                                root(j * 2 - 1, 1, HALF)
                            for k in {2: (0, 1), 3: (2,), 4: (3,), 5: (4,)}.get(i, ()):
                                norm(j * TEN + (k - HALF), j * 2 - 1, HALF + k)
                        if i == 8:
                            root(j * 2, 0, HALF)
                        for k in {9: (0, 1), 10: (2, 3, 4)}.get(i, ()):
                            norm(j * TEN + k, j * 2, k)

                round_(0)
                round_(1)
                with act.Fori(2, ITER) as j:
                    round_(j)
                root(ITER * 2 - 1, 1, HALF)
                for k in range(HALF):
                    norm(NT - HALF + k, ITER * 2 - 1, HALF + k)
                copy_x(NT, 0)
                root(ITER * 2, 0, 1)
                norm(NT, ITER * 2, 0)

            @block.vector
            def _(dve):
                v = nc.vector

                def first(t, i):
                    s, k = i // HALF, i % HALF
                    dve.wait_ge(p_ready, t + 1)
                    if after(t, TEN) and k == 0:
                        dve.wait_ge(h_out[s], (t - i) // TEN * 16 if isinstance(t, int) else hround[0] * 16)
                        dve.wait_ge(o_done, t - HALF)
                    v.scalar_tensor_tensor(out=H[s][:, k, :], in0=bank[2 + i % HALF][:, 0:D],
                                           scalar=omg_n[:, bass.ds(t, 1)], in1=X[s][:, k, :], op0=ALU.mult,
                                           op1=ALU.add).then_inc(a_done, 1)

                def add(t, i):
                    s, k = i // HALF, i % HALF
                    dve.wait_ge(a_done, t + 1)
                    v.scalar_tensor_tensor(out=H[s][:, k, :], in0=bank[2 + i % HALF][:, D:2 * D],
                                           scalar=gate_n[:, bass.ds(t, 1)], in1=H[s][:, k, :], op0=ALU.mult,
                                           op1=ALU.add).then_inc(h_done, 1)

                def stat(t, i):
                    s, k = i // HALF, i % HALF
                    dve.wait_ge(h_done, t + 1)
                    v.bn_stats(stats[:, i, :], H[s][:, k, :]).then_inc(s_done, 1)

                def variances(t_end, half, s, n):
                    dve.wait_ge(s_done, t_end)
                    dve.sem_inc(dve_hop, 1)
                    for k in range(n):
                        ins = v.bn_aggr(mv[:, s * HALF + k, :], stats[:, s * HALF + k, :])
                    ins.then_inc(mv_done, 1)
                    dve.wait_ge(mv_done, half + 1)
                    v.tensor_scalar(var_s[:, s * HALF:s * HALF + n], mv[:, s * HALF:s * HALF + n, 1], 1.0 + EPS,
                                    EPS * EPS, ALU.mult, ALU.add).then_inc(var_ready, 1)

                def scales(half, s, n):
                    sl = slice(s * HALF, s * HALF + n)
                    dve.wait_ge(sd_ready, half + 1)
                    v.reciprocal(r_s[:, sl], sd_s[:, sl]).then_inc(r_done, 1)
                    dve.wait_ge(r_done, half + 1)
                    v.scalar_tensor_tensor(out=nb_s[:, sl], in0=mv[:, sl, 0], scalar=-1.0, in1=r_s[:, sl],
                                           op0=ALU.mult, op1=ALU.mult).then_inc(nb_ready, 1)

                hround = [0]

                def round_(j):
                    hround[0] = j
                    for i in range(TEN):
                        if i < TEN:
                            first(j * TEN + i, i)
                        if i == 0 and later(j):
                            stat(j * TEN - 1, TEN - 1)
                            variances(j * TEN, j * 2 - 1, 1, HALF)
                        elif i:
                            stat(j * TEN + (i - 1), i - 1)
                        if i < TEN:
                            add(j * TEN + i, i)
                        if i == 2 and later(j):
                            scales(j * 2 - 1, 1, HALF)
                        if i == 5:
                            variances(j * TEN + HALF, j * 2, 0, HALF)
                        if i == 8:
                            scales(j * 2, 0, HALF)

                round_(0)
                round_(1)
                with dve.Fori(2, ITER) as j:
                    round_(j)
                stat(NT - 1, TEN - 1)
                variances(NT, ITER * 2 - 1, 1, HALF)
                scales(ITER * 2 - 1, 1, HALF)
                hround[0] = ITER
                first(NT, 0)
                add(NT, 0)
                stat(NT, 0)
                variances(NT + 1, ITER * 2, 0, 1)
                scales(ITER * 2, 0, 1)

            @block.tensor
            def _(pe):
                t_ = nc.tensor

                def turn(t, i, jx):
                    s, k = i // HALF, i % HALF
                    if k == 0:
                        pe.wait_ge(x_in[s], jx * 16 + 16)
                    if after(t, 2):
                        pe.wait_ge(xt_copied, t - 1)
                    for c in range(2):
                        ins = t_.transpose(bank[i % 2][:, c * P:(c + 1) * P], X[s][:, k, c * P:(c + 1) * P],
                                           ident[:, :])
                    ins.then_inc(xt_ready, 1)

                def product(t, i):
                    if after(t, HALF):
                        pe.wait_ge(h_done, t - (HALF - 1))
                    p = bank[2 + i % HALF]
                    t_.matmul(p[:, :], ones3[:, :], bias3[:, 0:NB], start=True, stop=False, skip_group_check=True)
                    pe.wait_ge(xt_copied, t + 1)
                    for c in range(2):
                        ins = t_.matmul(p[:, 0:384], xT[i % 2][:, c * P:(c + 1) * P], w_node[:, c, :], start=False,
                                        stop=c == 1, skip_group_check=True)
                    ins.then_inc(p_ready, 1)

                def round_(j):
                    for i in range(TEN + 1):
                        if i < TEN:
                            turn(j * TEN + i, i, j)
                        if i:
                            product(j * TEN + (i - 1), i - 1)

                round_(0)
                round_(1)
                with pe.Fori(2, ITER) as j:
                    round_(j)
                turn(NT, 0, ITER)
                product(NT, 0)

        give_back()

        SL = 8
        TAKEN = 16 // SL
        SLOTS = [len(range(q, ET, SL)) for q in range(SL)]
        ek = sb("ek", [P, ET, 8])
        e_idx = sb("e_idx", [P, SL, 4], I32)
        e_key = sb("e_key", [P, SL, 8])
        eq = [sb(f"eq{b}", [P, 2, P]) for b in range(2)]
        tot = [sb(f"tot{b}", [P, D + HEADS]) for b in range(2)]
        same = tmp("same", [P, ET])
        xg = [tmp(f"xg{q}", [P, D + 1]) for q in range(SL)]
        hg = [tmp(f"hg{q}", [P, D]) for q in range(SL)]
        hn = [tmp(f"hn{q}", [P, D]) for q in range(SL)]
        rc = [tmp(f"rc{b}", [P, 2]) for b in range(2)]
        mean = [tmp(f"mean{b}", [P, D]) for b in range(2)]
        meanT = [tmp(f"meanT{b}", [P, D]) for b in range(2)]
        rec_in, tab_ready, dve3, act3 = sem("rec_in"), sem("tab_ready"), sem("dve3"), sem("act3")
        i_full = sem("i_full")
        xg_in = [sem(f"xg_in{q}") for q in range(SL)]
        hg_in = [sem(f"hg_in{q}") for q in range(SL)]
        hn_out = [sem(f"hn_out{q}") for q in range(SL)]
        k_full, rb_ready, eq_ready, acc_ready, tot_ready = (sem(n) for n in (
            "k_full", "rb_ready", "eq_ready", "acc_ready", "tot_ready"))
        deg_ready, rc_ready, mean_ready, mt_ready, mt_copied, nb_prod, half_sum, hn_ready = (sem(n) for n in (
            "deg_ready", "rc_ready", "mean_ready", "mt_ready", "mt_copied", "nb_prod", "half_sum", "hn_ready"))

        with nc.Block() as block:
            @block.sync
            def _(sp):
                flat = rec_tab.rearrange("(p t) f -> p t f", p=P)
                sp.dma_start(rec[:, :, :], flat).then_inc(rec_in, 16)
                sp.dma_start(nxt[0:P - 1, :, :], flat[1:P]).then_inc(rec_in, 16)
                sp.dma_start(nxt[P - 1:P, 0:ET - 1, :], flat[0:1, 1:ET, :]).then_inc(rec_in, 16)
                sp.dma_start(nxt[P - 1:P, ET - 1:ET, :], flat[0:1, 0:1, :]).then_inc(rec_in, 16)
                sp.wait_ge(rec_in, 64)

            @block.scalar
            def _(act):
                a = nc.scalar
                act.wait_ge(rec_in, 64)
                a.activation(gate_e[:, :, 1], rec[:, :, 3], ACT.Sigmoid, bias=gwb[:, 1:2], scale=gwb[:, 0:1])\
                    .then_inc(act3, 1)
                act.wait_ge(act3, 1)
                a.activation(gate_e[:, :, 0], gate_e[:, :, 1], ACT.Copy, bias=1.0, scale=-1.0).then_inc(act3, 1)

                def total(t, q):
                    b = q % 2
                    act.wait_ge(acc_ready, t + 1)
                    if after(t, 2):
                        act.wait_ge(mean_ready, t - 1)
                    a.activation(tot[b][:, 0:D + 1], bank[2 + b][:, 0:D + 1], ACT.Copy).then_inc(tot_ready, 1)

                def divide(t, q):
                    b = q % 2
                    act.wait_ge(rc_ready, t + 1)
                    if after(t, 2):
                        act.wait_ge(mt_ready, t - 1)
                    a.activation(mean[b][:, :], tot[b][:, 0:D], ACT.Copy, scale=rc[b][:, 1:2])\
                        .then_inc(mean_ready, 1)

                def copy_mean(t, q):
                    b = q % 2
                    act.wait_ge(mt_ready, t + 1)
                    if after(t, 2):
                        act.wait_ge(nb_prod, t - 1)
                    a.activation(meanT[b][:, :], bank[4 + b][:, 0:D], ACT.Copy).then_inc(mt_copied, 1)

                skewed(act, ET, SL, [(total, 2), (divide, 3), (copy_mean, 4)])

            @block.gpsimd
            def _(pool):
                g = nc.gpsimd
                last = pool.to_reg(N - 1)
                pool.wait_ge(tab_ready, 1)

                def fetch(t, q):
                    if after(t, SL):
                        pool.wait_ge(hn_out[q], (t - q) * TAKEN)
                        pool.wait_ge(acc_ready, t - (SL - 1))
                        pool.wait_ge(half_sum, t - (SL - 1))
                    pool.sem_inc(pool_hop, 1)
                    g.tensor_copy(e_idx[:, q, :], idx_s[:, bass.ds(t, 1), :]).then_inc(i_full, 1)
                    pool.wait_ge(i_full, t + 1)
                    pool.sem_inc(pool_hop, 1)
                    g.indirect_dma_start(out=xg[q][:, 0:D], out_offset=None, in_=x,
                                         in_offset=bass.IndirectOffsetOnAxis(e_idx[:, q, 0:1], 0))\
                        .then_inc(xg_in[q], 16)
                    g.indirect_dma_start(out=hg[q][:, :], out_offset=None, in_=h_tab,
                                         in_offset=bass.IndirectOffsetOnAxis(e_idx[:, q, 1:2], 0),
                                         bounds_check=last, oob_is_err=False).then_inc(hg_in[q], 16)

                def put(t, q):
                    pool.wait_ge(hn_ready, t + 1)
                    pool.sem_inc(pool_hop, 1)
                    g.indirect_dma_start(out=h_tab, out_offset=bass.IndirectOffsetOnAxis(e_idx[:, q, 2:3], 0),
                                         in_=hn[q][:, :], in_offset=None, bounds_check=last, oob_is_err=False)\
                        .then_inc(hn_out[q], 16)

                skewed(pool, ET, SL, [(put, 7), (fetch, 0)])
                for q in range(SL):
                    pool.wait_ge(hn_out[q], SLOTS[q] * 16)

            @block.vector
            def _(dve):
                v = nc.vector
                st = Steps(dve, dve3)
                dve.wait_ge(rec_in, 64)
                for q in range(SL):
                    st.done(v.memset(xg[q][:, :], 1.0))
                    st.done(v.memset(hg[q][:, :], 0.0))
                st.done(v.memset(ek[:, :, :], 0.0))
                st.done(v.memset(prev1[:, :], 0.0))
                st.done(v.memset(idx_s[:, :, :], 0))
                st.done(v.tensor_scalar(key1[:, :], rec[:, :, 0], 1.0, None, ALU.add))
                st.done(v.tensor_tensor(same[:, :], rec[:, :, 0], nxt[:, :, 0], ALU.is_equal))
                st.wait()
                st.done(v.tensor_scalar(prev1[:, 1:ET], key1[:, 0:ET - 1], is127[:, :], None, ALU.mult))
                st.done(v.tensor_copy(idx_s[:, :, 0], rec[:, :, 1]))
                st.done(v.tensor_copy(idx_s[:, :, 1], rec[:, :, 0]))
                st.done(v.scalar_tensor_tensor(out=same[:, :], in0=same[:, :], scalar=PAD, in1=rec[:, :, 0],
                                               op0=ALU.mult, op1=ALU.add))
                st.wait()
                st.done(v.tensor_copy(idx_s[:, :, 2], same[:, :]))
                st.done(v.tensor_copy(ek[:, :, 0], key1[:, :]))
                st.done(v.tensor_copy(ek[:, :, 1], prev1[:, :]))
                dve.wait_ge(act3, 2)
                st.done(v.tensor_copy(ek[:, :, 2:4], gate_e[:, :, :]))
                st.wait()
                dve.sem_inc(tab_ready, 1)

                def keys_in(t, q):
                    if after(t, SL):
                        dve.wait_ge(hn_ready, t - (SL - 1))
                    v.tensor_copy(e_key[:, q, :], ek[:, bass.ds(t, 1), :]).then_inc(k_full, 1)

                def equal(t, q):
                    b = q % 2
                    dve.wait_ge(rb_ready, t + 1)
                    if after(t, 2):
                        dve.wait_ge(acc_ready, t - 1)
                    v.tensor_tensor(eq[b][:, :, :], bank[b][:, 0:P].unsqueeze(1).to_broadcast([P, 2, P]),
                                    e_key[:, q, 0:2].unsqueeze(2).to_broadcast([P, 2, P]), ALU.is_equal)\
                        .then_inc(eq_ready, 1)

                def divisor(t, q):
                    b = q % 2
                    dve.wait_ge(tot_ready, t + 1)
                    if after(t, 2):
                        dve.wait_ge(mean_ready, t - 1)
                    v.tensor_scalar(rc[b][:, 0:1], tot[b][:, D:D + 1], 1.0, None, ALU.max).then_inc(deg_ready, 1)
                    dve.wait_ge(deg_ready, t + 1)
                    v.reciprocal(rc[b][:, 1:2], rc[b][:, 0:1]).then_inc(rc_ready, 1)

                def join(t, q):
                    b = q % 2
                    dve.wait_ge(nb_prod, t + 1)
                    dve.wait_ge(hg_in[q], (t - q) * TAKEN + 16)
                    if after(t, SL):
                        dve.wait_ge(hn_out[q], (t - q) * TAKEN)
                    v.scalar_tensor_tensor(out=hn[q][:, :], in0=bank[6 + b][:, 0:D], scalar=e_key[:, q, 2:3],
                                           in1=hg[q][:, :], op0=ALU.mult, op1=ALU.add).then_inc(half_sum, 1)
                    dve.wait_ge(half_sum, t + 1)
                    v.scalar_tensor_tensor(out=hn[q][:, P:D], in0=bank[6 + b][:, D:D + P],
                                           scalar=e_key[:, q, 3:4], in1=hn[q][:, P:D], op0=ALU.mult,
                                           op1=ALU.add).then_inc(hn_ready, 1)

                skewed(dve, ET, SL, [(keys_in, 0), (equal, 1), (divisor, 3), (join, 6)])

            @block.tensor
            def _(pe):
                t_ = nc.tensor

                def rows(t, q):
                    b = q % 2
                    pe.wait_ge(k_full, t + 1)
                    if after(t, 2):
                        pe.wait_ge(eq_ready, t - 1)
                    t_.transpose(bank[b][:, 0:P], e_key[:, q, 0:1].to_broadcast([P, P]), ident[:, :])\
                        .then_inc(rb_ready, 1)

                def sums(t, q):
                    b = q % 2
                    pe.wait_ge(eq_ready, t + 1)
                    pe.wait_ge(xg_in[q], (t - q) * TAKEN + 16)
                    if after(t, 2):
                        pe.wait_ge(tot_ready, t - 1)
                    ins = t_.matmul(bank[2 + b][:, 0:D + 1], eq[b][:, 0, :], xg[q][:, :], start=True,
                                    stop=not after(t, 1))
                    if after(t, 1):
                        pe.wait_ge(tot_ready, t)
                        ins = t_.matmul(bank[2 + b][:, 0:D + 1], eq[b][:, 1, :], tot[1 - b][:, 0:D + 1],
                                        start=False, stop=True)
                    ins.then_inc(acc_ready, 1)

                def turn(t, q):
                    b = q % 2
                    pe.wait_ge(mean_ready, t + 1)
                    if after(t, 2):
                        pe.wait_ge(mt_copied, t - 1)
                    for c in range(2):
                        ins = t_.transpose(bank[4 + b][:, c * P:(c + 1) * P], mean[b][:, c * P:(c + 1) * P],
                                           ident[:, :])
                    ins.then_inc(mt_ready, 1)

                def product(t, q):
                    b = q % 2
                    pe.wait_ge(mt_copied, t + 1)
                    if after(t, 2):
                        pe.wait_ge(hn_ready, t - 1)
                    for c in range(2):
                        ins = t_.matmul(bank[6 + b][:, 0:384], meanT[b][:, c * P:(c + 1) * P], w_nb[:, c, :],
                                        start=c == 0, stop=c == 1)
                    ins.then_inc(nb_prod, 1)

                skewed(pe, ET, SL, [(rows, 0), (sums, 2), (turn, 4), (product, 5)])

        give_back()

        US = ET // 2
        u_idx = tmp("u_idx", [P, 2, 2, 4], I32)
        u_h = [tmp(f"u_h{s}", [P, 4, D]) for s in range(2)]
        u_x = [tmp(f"u_x{s}", [P, 4, D]) for s in range(2)]
        u_st = tmp("u_st", [P, 4, 6])
        u_mv = [tmp(f"u_mv{s}", [P, 4, 2]) for s in range(2)]
        u_var = tmp("u_var", [P, 4])
        u_sd = tmp("u_sd", [P, 4])
        u_r = tmp("u_r", [P, 4])
        u_nb = tmp("u_nb", [P, 4])
        xh = tmp("xh", [P, 2, 512], F32R)
        xl = tmp("xl", [P, 2, 512], F32R)
        hidT = [tmp(f"hidT{m}", [P, 512]) for m in range(8)]
        catT = [tmp(f"catT{k}", [P, 2, 2, P]) for k in range(2)]
        feat = [tmp(f"feat{s}", [P, 2, D]) for s in range(2)]
        att = tmp("att", [P, AB])
        ajunk = tmp("ajunk", [P, AB])
        e_slot = tmp("e_slot", [P, 2, 2])
        d_slot = tmp("d_slot", [P, 2, HEADS])
        u_full = sem("u_full")
        u_in = [sem(f"u_in{s}") for s in range(2)]
        names = ("v_stat v_mv v_var v_sd v_r v_nb v_x t_ready t_high t_low w1_ready act_hid dve_hid w2_ready "
                 "cat_ready f_turned f_ready a_ready at_read dots_done sc_done el_full").split()
        (v_stat, v_mv, v_var, v_sd, v_r, v_nb, v_x, t_ready, t_high, t_low, w1_ready, act_hid, dve_hid, w2_ready,
         cat_ready, f_turned, f_ready, a_ready, at_read, dots_done, sc_done, el_full) = (sem(n) for n in names)
        x_out = [sem(f"x_out{s}") for s in range(2)]
        f_out = [sem(f"f_out{s}") for s in range(2)]

        with nc.Block() as block:
            @block.gpsimd
            def _(pool):
                g = nc.gpsimd
                last = pool.to_reg(N - 1)

                def fetch(u, s):
                    if after(u, 2):
                        pool.wait_ge(u_in[s], (u - s) * 32)
                        pool.wait_ge(v_x, u * 4 - 4)
                    pool.sem_inc(pool_hop, 1)
                    g.tensor_copy(u_idx[:, s, :, :], idx_s[:, bass.ds(u * 2, 2), :]).then_inc(u_full, 1)
                    pool.wait_ge(u_full, u + 1)
                    pool.sem_inc(pool_hop, 1)
                    for b in range(2):
                        g.indirect_dma_start(out=u_h[s][:, b, :], out_offset=None, in_=h_tab,
                                             in_offset=bass.IndirectOffsetOnAxis(u_idx[:, s, b, 1:2], 0),
                                             bounds_check=last, oob_is_err=False).then_inc(u_in[s], 16)
                        g.indirect_dma_start(out=u_h[s][:, 2 + b, :], out_offset=None, in_=h_tab,
                                             in_offset=bass.IndirectOffsetOnAxis(u_idx[:, s, b, 0:1], 0))\
                            .then_inc(u_in[s], 16)

                skewed(pool, US, 2, [(fetch, 0)])

            @block.sync
            def _(sp):
                def keep_x(u, s):
                    sp.wait_ge(v_x, u * 4 + 4)
                    sp.dma_start(edge_tab[bass.ds(u * 2, 2), :, 0:D].rearrange("b p d -> p b d"),
                                 u_x[s][:, 0:2, :]).then_inc(x_out[s], 16)

                def keep_f(u, s):
                    sp.wait_ge(f_ready, u * 2 + 2)
                    sp.dma_start(edge_tab[bass.ds(u * 2, 2), :, D:2 * D].rearrange("b p d -> p b d"),
                                 feat[s][:, :, :]).then_inc(f_out[s], 16)

                skewed(sp, US, 2, [(keep_x, 0), (keep_f, 1)])
                for s in range(2):
                    sp.wait_ge(x_out[s], US // 2 * 16)
                    sp.wait_ge(f_out[s], US // 2 * 16)

            @block.scalar
            def _(act):
                a = nc.scalar

                def root(u, s):
                    act.wait_ge(v_var, u + 1)
                    a.activation(u_sd[:, :], u_var[:, :], ACT.Sqrt).then_inc(v_sd, 1)

                def norm(u, s):
                    act.wait_ge(v_nb, u + 1)
                    if after(u, 2):
                        act.wait_ge(t_ready, u - 1)
                        act.wait_ge(x_out[s], (u - s) * 8)
                    for k in range(4):
                        a.activation(u_x[s][:, k, :], u_h[s][:, k, :], ACT.Identity, bias=u_nb[:, k:k + 1],
                                     scale=u_r[:, k:k + 1]).then_inc(v_x, 1)

                def high(u, s):
                    act.wait_ge(t_ready, u + 1)
                    if after(u, 1):
                        act.wait_ge(w1_ready, u * 8)
                    for c in range(2):
                        a.activation(xh[:, c, :], bank[c][:, :], ACT.Copy).then_inc(t_high, 1)

                def relu(u, m):
                    act.wait_ge(w1_ready, u * 8 + (m + 1))
                    if m == 0 and after(u, 1):
                        act.wait_ge(w2_ready, u * 2)
                    a.activation(hidT[m][:, :], bank[2 + m % 2][:, :], ACT.Relu, bias=b1c[:, m:m + 1])\
                        .then_inc(act_hid, 1)

                def features(u, k):
                    act.wait_ge(w2_ready, u * 2 + (k + 1))
                    if after(u, 1):
                        act.wait_ge(a_ready, u * 2)
                    for h in range(2):
                        a.activation(catT[k][:, h, :, :], bank[4 + k][:, h * 2 * P:(h + 1) * 2 * P]
                                     .rearrange("p (b e) -> p b e", b=2), ACT.Identity,
                                     bias=b2c[:, 2 * k + h:2 * k + h + 1]).then_inc(cat_ready, 1)

                def step(u, s):
                    for m in (0, 2, 4, 6):
                        relu(u, m)

                def both(u, s):
                    for k in range(2):
                        features(u, k)

                skewed(act, US, 2, [(root, 0), (step, 2), (high, 1), (norm, 0), (both, 2)])

            @block.vector
            def _(dve):
                v = nc.vector

                def stat(u, s):
                    dve.wait_ge(u_in[s], (u - s) * 32 + 64)
                    for k in range(4):
                        v.bn_stats(u_st[:, k, :], u_h[s][:, k, :]).then_inc(v_stat, 1)
                    dve.wait_ge(v_stat, u * 4 + 4)
                    dve.sem_inc(dve_hop, 1)
                    for k in range(4):
                        v.bn_aggr(u_mv[s][:, k, :], u_st[:, k, :]).then_inc(v_mv, 1)
                    dve.wait_ge(v_mv, u * 4 + 4)
                    v.tensor_scalar(u_var[:, :], u_mv[s][:, :, 1], EPS, None, ALU.add).then_inc(v_var, 1)

                def scale(u, s):
                    dve.wait_ge(v_sd, u + 1)
                    if after(u, 1):
                        dve.wait_ge(v_x, u * 4)
                    v.reciprocal(u_r[:, :], u_sd[:, :]).then_inc(v_r, 1)
                    dve.wait_ge(v_r, u + 1)
                    v.scalar_tensor_tensor(out=u_nb[:, :], in0=u_mv[s][:, :, 0], scalar=-1.0, in1=u_r[:, :],
                                           op0=ALU.mult, op1=ALU.mult).then_inc(v_nb, 1)

                def relu(u, m):
                    dve.wait_ge(w1_ready, u * 8 + (m + 1))
                    v.tensor_scalar(hidT[m][:, :], bank[2 + m % 2][:, :], b1c[:, m:m + 1], 0.0, ALU.add, ALU.max)\
                        .then_inc(dve_hid, 1)

                def low(u, s):
                    for c in range(2):
                        dve.wait_ge(t_high, u * 2 + (c + 1))
                        v.tensor_tensor(xl[:, c, :], bank[c][:, :], xh[:, c, :].bitcast(F32), ALU.subtract)\
                            .then_inc(t_low, 1)

                def copy_feat(u, s, k):
                    dve.wait_ge(f_turned, u * 2 + (k + 1))
                    if after(u, 2) and k == 0:
                        dve.wait_ge(f_out[s], (u - s) * 8)
                    v.tensor_copy(feat[s][:, :, k * P:(k + 1) * P].rearrange("p b (h f) -> p h b f", h=2),
                                  bank[4 + k][:, :].rearrange("p (h b f) -> p h b f", h=2, b=2)[:, :, :, FEAT:P])\
                        .then_inc(f_ready, 1)

                def dots(u, b):
                    v.tensor_copy(e_slot[:, b, 0:1], rec[:, bass.ds(u * 2 + b, 1), 2]).then_inc(el_full, 1)
                    dve.wait_ge(el_full, u * 2 + (b + 1))
                    dve.wait_ge(a_ready, u * 2 + (b + 1))
                    for k in range(2):
                        o = k * (AB // 2)
                        v.scalar_tensor_tensor(out=att[:, o:o + AB // 2], in0=a1e[:, o:o + AB // 2],
                                               scalar=e_slot[:, b, 0:1], in1=bank[6 + k][:, 0:AB // 2],
                                               op0=ALU.mult, op1=ALU.add).then_inc(at_read, 1)
                    dve.wait_ge(at_read, u * 4 + (2 * b + 2))
                    for h in range(HEADS):
                        sl = slice(h * ATT, (h + 1) * ATT)
                        v.scalar_tensor_tensor(out=ajunk[:, sl], in0=att[:, sl], scalar=0.0, in1=a2b[:, sl],
                                               op0=ALU.max, op1=ALU.mult, accum_out=d_slot[:, b, h:h + 1])\
                            .then_inc(dots_done, 1)
                    dve.wait_ge(dots_done, u * 8 + (4 * b + 4))
                    v.tensor_copy(score[:, bass.ds(u * 2 + b, 1), :], d_slot[:, b, :]).then_inc(sc_done, 1)

                def step(u, s):
                    relu(u, 1)
                    if after(u, 1):
                        copy_feat(u - 1, 1 - s, 0)
                    relu(u, 3)
                    if after(u, 1):
                        dots(u - 1, 0)
                        copy_feat(u - 1, 1 - s, 1)
                    relu(u, 5)
                    if after(u, 1):
                        dots(u - 1, 1)
                    relu(u, 7)

                def tail(u, s):
                    if isinstance(u, int) and u == US - 1:
                        for b in range(2):
                            copy_feat(u, s, b)
                            dots(u, b)

                skewed(dve, US, 2, [(stat, 0), (step, 2), (low, 1), (scale, 0), (tail, 2)])

            @block.tensor
            def _(pe):
                t_ = nc.tensor

                def turn(u, s):
                    pe.wait_ge(v_x, u * 4 + 4)
                    if after(u, 1):
                        pe.wait_ge(t_low, u * 2)
                    for c in range(2):
                        for k in range(4):
                            ins = t_.transpose(bank[c][:, k * P:(k + 1) * P], u_x[s][:, k, c * P:(c + 1) * P],
                                               ident[:, :])
                    ins.then_inc(t_ready, 1)

                def hidden(u, m):
                    pe.wait_ge(t_low, u * 2 + 2)
                    if m > 1:
                        pe.wait_ge(act_hid if m % 2 == 0 else dve_hid, u * 4 + m // 2)
                    elif after(u, 1):
                        pe.wait_ge(act_hid if m % 2 == 0 else dve_hid, u * 4)
                    n = 0
                    for w, xx in ((w1h, xh), (w1l, xh), (w1h, xl)):
                        for c in range(2):
                            ins = t_.matmul(bank[2 + m % 2][:, :], w[:, c, m * P:(m + 1) * P], xx[:, c, :],
                                            start=n == 0, stop=n == 5)
                            n += 1
                    ins.then_inc(w1_ready, 1)

                def features(u, k):
                    if k == 0:
                        pe.wait_ge(act_hid, u * 4 + 4)
                        pe.wait_ge(dve_hid, u * 4 + 4)
                    if after(u, 1):
                        pe.wait_ge(f_ready, u * 2 - 1 + k)
                    for h in range(2):
                        for c in range(2):
                            m = 2 * (2 * k + h) + c
                            for side in range(2):
                                ins = t_.matmul(bank[4 + k][side * FEAT:(side + 1) * FEAT, h * 2 * P:(h + 1) * 2 * P],
                                                w2f[:, m, :], hidT[m][:, side * 2 * P:(side + 1) * 2 * P],
                                                start=c == 0, stop=c == 1, skip_group_check=True)
                    ins.then_inc(w2_ready, 1)

                def turn_feat(u, k):
                    pe.wait_ge(cat_ready, u * 4 + (2 * k + 2))
                    for h in range(2):
                        for b in range(2):
                            o = (2 * h + b) * P
                            ins = t_.transpose(bank[4 + k][:, o:o + P], catT[k][:, h, b, :], ident[:, :])
                    ins.then_inc(f_turned, 1)

                def scores(u, b):
                    pe.wait_ge(cat_ready, u * 4 + 4)
                    if b or after(u, 1):
                        pe.wait_ge(at_read, u * 4 + 2 * b)
                    for k in range(2):
                        o = NB + k * (AB // 2)
                        t_.matmul(bank[6 + k][:, 0:AB // 2], ones3[:, :], bias3[:, o:o + AB // 2], start=True,
                                  stop=False, skip_group_check=True)
                        for h in range(2):
                            ins = t_.matmul(bank[6 + k][:, h * ATT:(h + 1) * ATT], catT[k][:, h, b, :],
                                            a1f[:, 2 * k + h, :], start=False, stop=h == 1, skip_group_check=True)
                    ins.then_inc(a_ready, 1)

                def step(u, s):
                    hidden(u, 0)
                    hidden(u, 1)
                    if after(u, 1):
                        turn_feat(u - 1, 0)
                    hidden(u, 2)
                    if after(u, 1):
                        scores(u - 1, 0)
                    hidden(u, 3)
                    if after(u, 1):
                        turn_feat(u - 1, 1)
                    hidden(u, 4)
                    if after(u, 1):
                        scores(u - 1, 1)
                    hidden(u, 5)
                    hidden(u, 6)
                    hidden(u, 7)

                def both(u, s):
                    features(u, 0)
                    features(u, 1)

                def tail(u, s):
                    if isinstance(u, int) and u == US - 1:
                        for b in range(2):
                            turn_feat(u, b)
                            scores(u, b)

                skewed(pe, US, 2, [(step, 1), (turn, 0), (both, 1), (tail, 1)])

        give_back()

        raw = tmp("raw", [P, ET, HEADS])
        mx = tmp("mx", [P, HEADS])
        mxa = tmp("mxa", [P, HEADS])
        er = [tmp(f"er{q}", [P, 2 * D]) for q in range(SL)]
        val = [tmp(f"val{q}", [P, D + HEADS]) for q in range(SL)]
        z = [tmp(f"z{q}", [P, D]) for q in range(SL)]
        zo = [tmp(f"zo{q}", [P, D]) for q in range(SL)]
        rs = tmp("rs", [P, 2, 2 * HEADS])
        z_st, z_mv = tmp("z_st", [P, 2, 6]), tmp("z_mv", [P, SL, 2])
        z_s = tmp("z_s", [P, SL, 4])
        (dve5, mx_ready, mxa_ready, sub_done, w_ready, ek_done, k5_full, rb5, eq5, val_ready, acc5, tot5, den5,
         rs5, zs_ready, z_ready, zst, zmv, zvar, zsd, zr, znb, zo_ready, i5_full) = (sem(n) for n in (
             "dve5 mx_ready mxa_ready sub_done w_ready ek_done k5_full rb5_ready eq5_ready val_ready acc5_ready "
             "tot5_ready den_ready rs_ready zs_ready z_ready z_stat z_aggr z_var z_sd z_r z_nb zo_ready i5_full").split())
        er_in = [sem(f"er_in{q}") for q in range(SL)]
        zo_out = [sem(f"zo_out{q}") for q in range(SL)]

        with nc.Block() as block:
            @block.sync
            def _(sp):
                def load(t, q):
                    if after(t, SL):
                        sp.wait_ge(z_ready, t - (SL - 1))
                        sp.wait_ge(val_ready, t - (SL - 1))
                    sp.dma_start(er[q][:, :], edge_tab[bass.ds(t, 1)].rearrange("b p d -> (b p) d"))\
                        .then_inc(er_in[q], 16)

                skewed(sp, ET, SL, [(load, 0)])

            @block.gpsimd
            def _(pool):
                g = nc.gpsimd
                last = pool.to_reg(N - 1)
                pool.wait_ge(mx_ready, 1)
                g.partition_all_reduce(mxa[:, :], mx[:, :], P, bass.bass_isa.ReduceOp.max).then_inc(mxa_ready, 1)
                pool.wait_ge(ek_done, 1)

                def weigh(t, q):
                    pool.wait_ge(er_in[q], (t - q) * TAKEN + 16)
                    pool.wait_ge(k5_full, t + 1)
                    if after(t, SL):
                        pool.wait_ge(acc5, t - (SL - 1))
                    pool.sem_inc(pool_hop, 1)
                    g.tensor_copy(val[q][:, D:D + HEADS], e_key[:, q, 4:8])
                    g.tensor_tensor(val[q][:, 0:D].rearrange("p (h f) -> p h f", h=HEADS),
                                    er[q][:, D:2 * D].rearrange("p (h f) -> p h f", h=HEADS),
                                    e_key[:, q, 4:8].unsqueeze(2).to_broadcast([P, HEADS, FEAT]), ALU.mult)\
                        .then_inc(val_ready, 1)

                def index(t, q):
                    if after(t, SL):
                        pool.wait_ge(zo_out[q], (t - q) * TAKEN)
                    pool.sem_inc(pool_hop, 1)
                    g.tensor_copy(e_idx[:, q, :], idx_s[:, bass.ds(t, 1), :]).then_inc(i5_full, 1)

                def put(t, q):
                    pool.wait_ge(zo_ready, t + 1)
                    pool.wait_ge(i5_full, t + 1)
                    pool.sem_inc(pool_hop, 1)
                    g.indirect_dma_start(out=out, out_offset=bass.IndirectOffsetOnAxis(e_idx[:, q, 2:3], 0),
                                         in_=zo[q][:, :], in_offset=None, bounds_check=last, oob_is_err=False)\
                        .then_inc(zo_out[q], 16)

                skewed(pool, ET, SL, [(weigh, 0), (index, 3), (put, 7)])
                for q in range(SL):
                    pool.wait_ge(zo_out[q], SLOTS[q] * 16)

            @block.scalar
            def _(act):
                a = nc.scalar
                act.wait_ge(sub_done, 1)
                a.activation(wgt[:, :, :], raw[:, :, :], ACT.Exp).then_inc(w_ready, 1)

                def total(t, q):
                    b = q % 2
                    act.wait_ge(acc5, t + 1)
                    if after(t, 2):
                        act.wait_ge(zs_ready, (t - 1) * HEADS)
                    a.activation(tot[b][:, :], bank[2 + b][:, 0:D + HEADS], ACT.Copy).then_inc(tot5, 1)

                def divide(t, q):
                    b = q % 2
                    act.wait_ge(rs5, t + 1)
                    if after(t, SL):
                        act.wait_ge(zo_ready, t - (SL - 1))
                    for h in range(HEADS):
                        sl = slice(h * FEAT, (h + 1) * FEAT)
                        a.activation(z[q][:, sl], tot[b][:, sl], ACT.Copy, scale=rs[:, b, HEADS + h:HEADS + h + 1])\
                            .then_inc(zs_ready, 1)

                def root(t, q):
                    act.wait_ge(zvar, t + 1)
                    a.activation(z_s[:, q, 1:2], z_s[:, q, 0:1], ACT.Sqrt).then_inc(zsd, 1)

                def norm(t, q):
                    act.wait_ge(znb, t + 1)
                    if after(t, SL):
                        act.wait_ge(zo_out[q], (t - q) * TAKEN)
                    a.activation(zo[q][:, :], z[q][:, :], ACT.Identity, bias=z_s[:, q, 3:4],
                                 scale=z_s[:, q, 2:3]).then_inc(zo_ready, 1)

                skewed(act, ET, SL, [(total, 3), (root, 6), (divide, 4), (norm, 7)])

            @block.vector
            def _(dve):
                v = nc.vector
                st = Steps(dve, dve5)
                for h in range(HEADS):
                    st.done(v.tensor_scalar(score[:, :, h], score[:, :, h], ab2b[:, h:h + 1], None, ALU.add))
                st.wait()
                st.done(v.scalar_tensor_tensor(out=raw[:, :, :], in0=score[:, :, :], scalar=0.2,
                                               in1=score[:, :, :], op0=ALU.mult, op1=ALU.max))
                st.wait()
                st.done(v.tensor_reduce(mx[:, :], raw[:, 0:EC, :].rearrange("p t h -> p h t"), AX.X, ALU.max))
                st.wait()
                for p0 in range(0, ER, 32):
                    sl = slice(p0, min(ER, p0 + 32))
                    st.done(v.tensor_tensor(mx[sl, :], mx[sl, :], raw[sl, EC, :], ALU.max))
                st.wait()
                dve.sem_inc(mx_ready, 1)
                dve.wait_ge(mxa_ready, 1)
                for h in range(HEADS):
                    st.done(v.tensor_scalar(raw[:, :, h], raw[:, :, h], mxa[:, h:h + 1], 0.0, ALU.subtract,
                                            ALU.min))
                st.wait()
                dve.sem_inc(sub_done, 1)
                dve.wait_ge(w_ready, 1)
                v.tensor_copy(ek[:, :, 4:8], wgt[:, :, :]).then_inc(ek_done, 1)
                dve.wait_ge(ek_done, 1)

                def keys_in(t, q):
                    if after(t, SL):
                        dve.wait_ge(val_ready, t - (SL - 1))
                    v.tensor_copy(e_key[:, q, :], ek[:, bass.ds(t, 1), :]).then_inc(k5_full, 1)

                def equal(t, q):
                    b = q % 2
                    dve.wait_ge(rb5, t + 1)
                    if after(t, 2):
                        dve.wait_ge(acc5, t - 1)
                    v.tensor_tensor(eq[b][:, :, :], bank[b][:, 0:P].unsqueeze(1).to_broadcast([P, 2, P]),
                                    e_key[:, q, 0:2].unsqueeze(2).to_broadcast([P, 2, P]), ALU.is_equal)\
                        .then_inc(eq5, 1)

                def divisor(t, q):
                    b = q % 2
                    dve.wait_ge(tot5, t + 1)
                    if after(t, 2):
                        dve.wait_ge(zs_ready, (t - 1) * HEADS)
                    v.tensor_scalar(rs[:, b, 0:HEADS], tot[b][:, D:D + HEADS], 1e-10, None, ALU.add)\
                        .then_inc(den5, 1)

                def inverse(t, q):
                    b = q % 2
                    dve.wait_ge(den5, t + 1)
                    v.reciprocal(rs[:, b, HEADS:2 * HEADS], rs[:, b, 0:HEADS]).then_inc(rs5, 1)

                def join(t, q):
                    dve.wait_ge(zs_ready, (t + 1) * HEADS)
                    v.tensor_tensor(z[q][:, :], z[q][:, :], er[q][:, 0:D], ALU.add).then_inc(z_ready, 1)

                def stat(t, q):
                    dve.wait_ge(z_ready, t + 1)
                    v.bn_stats(z_st[:, q % 2, :], z[q][:, :]).then_inc(zst, 1)

                def aggr(t, q):
                    dve.wait_ge(zst, t + 1)
                    dve.sem_inc(dve_hop, 1)
                    v.bn_aggr(z_mv[:, q, :], z_st[:, q % 2, :]).then_inc(zmv, 1)

                def variance(t, q):
                    dve.wait_ge(zmv, t + 1)
                    v.tensor_scalar(z_s[:, q, 0:1], z_mv[:, q, 1:2], EPS, None, ALU.add).then_inc(zvar, 1)

                def scale(t, q):
                    dve.wait_ge(zsd, t + 1)
                    v.reciprocal(z_s[:, q, 2:3], z_s[:, q, 1:2]).then_inc(zr, 1)

                def shift(t, q):
                    dve.wait_ge(zr, t + 1)
                    v.scalar_tensor_tensor(out=z_s[:, q, 3:4], in0=z_mv[:, q, 0:1], scalar=-1.0,
                                           in1=z_s[:, q, 2:3], op0=ALU.mult, op1=ALU.mult).then_inc(znb, 1)

                skewed(dve, ET, SL, [(stat, 6), (keys_in, 0), (aggr, 6), (scale, 7), (equal, 2), (variance, 6),
                                     (divisor, 4), (shift, 7), (join, 5), (inverse, 4)])

            @block.tensor
            def _(pe):
                t_ = nc.tensor

                def rows(t, q):
                    b = q % 2
                    pe.wait_ge(k5_full, t + 1)
                    if after(t, 2):
                        pe.wait_ge(eq5, t - 1)
                    t_.transpose(bank[b][:, 0:P], e_key[:, q, 0:1].to_broadcast([P, P]), ident[:, :])\
                        .then_inc(rb5, 1)

                def sums(t, q):
                    b = q % 2
                    pe.wait_ge(eq5, t + 1)
                    pe.wait_ge(val_ready, t + 1)
                    if after(t, 2):
                        pe.wait_ge(tot5, t - 1)
                    ins = t_.matmul(bank[2 + b][:, 0:D + HEADS], eq[b][:, 0, :], val[q][:, :], start=True,
                                    stop=not after(t, 1))
                    if after(t, 1):
                        pe.wait_ge(tot5, t)
                        ins = t_.matmul(bank[2 + b][:, 0:D + HEADS], eq[b][:, 1, :], tot[1 - b][:, :],
                                        start=False, stop=True)
                    ins.then_inc(acc5, 1)

                skewed(pe, ET, SL, [(rows, 1), (sums, 3)])
        give_back()


_NAMES = {'x': 'x', 'src': 'src', 'dst': 'dst', 'edge_weight': 'edge_weight', 'node_vec': 'node_vec',
          'L0_gnn_W_mean': 'W_mean', 'L0_gnn_b_mean': 'b_mean', 'L0_gnn_W_ego': 'W_ego', 'L0_gnn_b_ego': 'b_ego',
          'L0_gnn_W_nb': 'W_nb', 'L0_gnn_b_nb': 'b_nb', 'L0_gnn_gate_weight': 'gate_weight',
          'L0_gnn_gate_bias': 'gate_bias', 'L1_gnn_W1': 'W1', 'L1_gnn_b1': 'b1', 'L1_gnn_W2': 'W2',
          'L1_gnn_b2': 'b2', 'L1_gnn_A1': 'A1', 'L1_gnn_ab1': 'ab1', 'L1_gnn_A2': 'A2', 'L1_gnn_ab2': 'ab2'}


def kernel(**inputs):
    import concourse.bacc as bacc
    from concourse.bass_utils import run_bass_kernel_spmd

    nc = bacc.Bacc("TRN2", target_bir_lowering=False, num_devices=1)
    arrays, aps = {}, {}
    for name, short in _NAMES.items():
        a = np.ascontiguousarray(inputs[name])
        if a.ndim == 0:
            a = a.reshape(1)
        arrays[f"in_{short}"] = a
        aps[short] = nc.dram_tensor(f"in_{short}", a.shape, mybir.dt.from_np(a.dtype), kind="ExternalInput").ap()
    shape = arrays["in_x"].shape
    aps["out"] = nc.dram_tensor("out_x", shape, F32, kind="ExternalOutput").ap()
    build(nc, **aps)
    r = run_bass_kernel_spmd(nc, [arrays], core_ids=[0])
    return r.results[0]["out_x"]
```
